# Optimizing a Trainium2 kernel written in Bass

```python
import numpy as np
import jax
import jax.numpy as jnp

def _softmax(x, axis=-1):
    return jax.nn.softmax(x, axis=axis)

def _gelu(x):
    return jax.nn.gelu(x, approximate=True)

def _silu(x):
    return jax.nn.silu(x)

def _sigmoid(x):
    return jax.nn.sigmoid(x)

def _layernorm(x, axis=-1, eps=1e-05):
    m = jnp.mean(x, axis=axis, keepdims=True)
    v = jnp.var(x, axis=axis, keepdims=True)
    return (x - m) / jnp.sqrt(v + eps)

def _scatter_add(tgt, idx, src, axis=0):
    return tgt.at[idx].add(src)

def _segment_sum(src, seg, n):
    return jax.ops.segment_sum(src, seg, n)
kernel_name = 'mk_dlrm_tower_d1_rec_r8_e1dac8'

def setup_inputs(seed: int=0):
    np.random.seed(seed)
    _w = jnp.asarray

    def _rec_inputs():
        import jax
        import jax.numpy as jnp
        _tk = jax.random.key(seed)
        ids = jnp.stack([jax.random.randint(jax.random.fold_in(_tk, 200 + f), (512,), 0, v, jnp.int32) for f, v in enumerate([1000, 1000, 125000, 12500, 1250, 1250, 1000, 1000, 1000, 1000, 1250, 1000, 1250, 1000, 1000, 1250, 12500, 1000, 12500, 1000, 12500, 1250, 1000, 1250, 1250, 1000])], axis=1)
        tbl_0 = 0.05 * jax.random.normal(jax.random.fold_in(_tk, 500 + 0), (1000, 128), jnp.float32)
        tbl_1 = 0.05 * jax.random.normal(jax.random.fold_in(_tk, 500 + 1), (1000, 128), jnp.float32)
        tbl_2 = 0.05 * jax.random.normal(jax.random.fold_in(_tk, 500 + 2), (125000, 128), jnp.float32)
        tbl_3 = 0.05 * jax.random.normal(jax.random.fold_in(_tk, 500 + 3), (12500, 128), jnp.float32)
        tbl_4 = 0.05 * jax.random.normal(jax.random.fold_in(_tk, 500 + 4), (1250, 128), jnp.float32)
        tbl_5 = 0.05 * jax.random.normal(jax.random.fold_in(_tk, 500 + 5), (1250, 128), jnp.float32)
        tbl_6 = 0.05 * jax.random.normal(jax.random.fold_in(_tk, 500 + 6), (1000, 128), jnp.float32)
        tbl_7 = 0.05 * jax.random.normal(jax.random.fold_in(_tk, 500 + 7), (1000, 128), jnp.float32)
        tbl_8 = 0.05 * jax.random.normal(jax.random.fold_in(_tk, 500 + 8), (1000, 128), jnp.float32)
        tbl_9 = 0.05 * jax.random.normal(jax.random.fold_in(_tk, 500 + 9), (1000, 128), jnp.float32)
        tbl_10 = 0.05 * jax.random.normal(jax.random.fold_in(_tk, 500 + 10), (1250, 128), jnp.float32)
        tbl_11 = 0.05 * jax.random.normal(jax.random.fold_in(_tk, 500 + 11), (1000, 128), jnp.float32)
        tbl_12 = 0.05 * jax.random.normal(jax.random.fold_in(_tk, 500 + 12), (1250, 128), jnp.float32)
        tbl_13 = 0.05 * jax.random.normal(jax.random.fold_in(_tk, 500 + 13), (1000, 128), jnp.float32)
        tbl_14 = 0.05 * jax.random.normal(jax.random.fold_in(_tk, 500 + 14), (1000, 128), jnp.float32)
        tbl_15 = 0.05 * jax.random.normal(jax.random.fold_in(_tk, 500 + 15), (1250, 128), jnp.float32)
        tbl_16 = 0.05 * jax.random.normal(jax.random.fold_in(_tk, 500 + 16), (12500, 128), jnp.float32)
        tbl_17 = 0.05 * jax.random.normal(jax.random.fold_in(_tk, 500 + 17), (1000, 128), jnp.float32)
        tbl_18 = 0.05 * jax.random.normal(jax.random.fold_in(_tk, 500 + 18), (12500, 128), jnp.float32)
        tbl_19 = 0.05 * jax.random.normal(jax.random.fold_in(_tk, 500 + 19), (1000, 128), jnp.float32)
        tbl_20 = 0.05 * jax.random.normal(jax.random.fold_in(_tk, 500 + 20), (12500, 128), jnp.float32)
        tbl_21 = 0.05 * jax.random.normal(jax.random.fold_in(_tk, 500 + 21), (1250, 128), jnp.float32)
        tbl_22 = 0.05 * jax.random.normal(jax.random.fold_in(_tk, 500 + 22), (1000, 128), jnp.float32)
        tbl_23 = 0.05 * jax.random.normal(jax.random.fold_in(_tk, 500 + 23), (1250, 128), jnp.float32)
        tbl_24 = 0.05 * jax.random.normal(jax.random.fold_in(_tk, 500 + 24), (1250, 128), jnp.float32)
        tbl_25 = 0.05 * jax.random.normal(jax.random.fold_in(_tk, 500 + 25), (1000, 128), jnp.float32)
        _rk = jax.random.fold_in(_tk, 7)
        r_dense = -0.000520686 + 1.00062 * jax.random.normal(jax.random.fold_in(_rk, 101), (512, 128), jnp.float32)
        W_top1 = 0.0456912 * jax.random.normal(jax.random.fold_in(_tk, 801), (479, 512), jnp.float32)
        W_top2 = 0.0441942 * jax.random.normal(jax.random.fold_in(_tk, 802), (512, 256), jnp.float32)
        W_top3 = 0.0625 * jax.random.normal(jax.random.fold_in(_tk, 803), (256, 1), jnp.float32)
        b_top1 = jnp.zeros((512,), jnp.float32)
        b_top2 = jnp.zeros((256,), jnp.float32)
        return (r_dense, ids, tbl_0, tbl_1, tbl_2, tbl_3, tbl_4, tbl_5, tbl_6, tbl_7, tbl_8, tbl_9, tbl_10, tbl_11, tbl_12, tbl_13, tbl_14, tbl_15, tbl_16, tbl_17, tbl_18, tbl_19, tbl_20, tbl_21, tbl_22, tbl_23, tbl_24, tbl_25, W_top1, b_top1, W_top2, b_top2, W_top3)
    r_dense, ids, tbl_0, tbl_1, tbl_2, tbl_3, tbl_4, tbl_5, tbl_6, tbl_7, tbl_8, tbl_9, tbl_10, tbl_11, tbl_12, tbl_13, tbl_14, tbl_15, tbl_16, tbl_17, tbl_18, tbl_19, tbl_20, tbl_21, tbl_22, tbl_23, tbl_24, tbl_25, W_top1, b_top1, W_top2, b_top2, W_top3 = _rec_inputs()

    def _L0_rec_setup():
        import jax, jax.numpy as jnp
        import numpy as np
        B, NUM_EMBS, D = (2048, 26, 128)
        key = jax.random.key(seed)
        k1, k2 = jax.random.split(key)
        dense = jax.random.normal(k1, (B, D), dtype=jnp.float32)
        embs = jax.random.normal(k2, (B, NUM_EMBS, D), dtype=jnp.float32)
        return {'dense': dense, 'embs': embs}
    _L0_rec_all = _L0_rec_setup()
    _L0_rec_in = {k: v for k, v in _L0_rec_all.items() if k in ()}
    del _L0_rec_all
    return {'r_dense': r_dense, 'ids': ids, 'tbl_0': tbl_0, 'tbl_1': tbl_1, 'tbl_2': tbl_2, 'tbl_3': tbl_3, 'tbl_4': tbl_4, 'tbl_5': tbl_5, 'tbl_6': tbl_6, 'tbl_7': tbl_7, 'tbl_8': tbl_8, 'tbl_9': tbl_9, 'tbl_10': tbl_10, 'tbl_11': tbl_11, 'tbl_12': tbl_12, 'tbl_13': tbl_13, 'tbl_14': tbl_14, 'tbl_15': tbl_15, 'tbl_16': tbl_16, 'tbl_17': tbl_17, 'tbl_18': tbl_18, 'tbl_19': tbl_19, 'tbl_20': tbl_20, 'tbl_21': tbl_21, 'tbl_22': tbl_22, 'tbl_23': tbl_23, 'tbl_24': tbl_24, 'tbl_25': tbl_25, 'W_top1': W_top1, 'b_top1': b_top1, 'W_top2': W_top2, 'b_top2': b_top2, 'W_top3': W_top3}

def reference(r_dense, ids, tbl_0, tbl_1, tbl_2, tbl_3, tbl_4, tbl_5, tbl_6, tbl_7, tbl_8, tbl_9, tbl_10, tbl_11, tbl_12, tbl_13, tbl_14, tbl_15, tbl_16, tbl_17, tbl_18, tbl_19, tbl_20, tbl_21, tbl_22, tbl_23, tbl_24, tbl_25, W_top1, b_top1, W_top2, b_top2, W_top3):
    import jax
    import jax.numpy as jnp

    def _L0_rec_ref(dense, embs):
        import jax, jax.numpy as jnp
        import numpy as np
        B, NUM_EMBS, D = (2048, 26, 128)
        T = jnp.concatenate([dense[:, None, :], embs], axis=1)
        N = T.shape[1]
        Z = jnp.einsum('bnd,bmd->bnm', T, T)
        iu0, iu1 = jnp.triu_indices(N, k=1)
        return Z[:, iu0, iu1]
    e = jnp.stack([tbl_0[ids[:, 0]], tbl_1[ids[:, 1]], tbl_2[ids[:, 2]], tbl_3[ids[:, 3]], tbl_4[ids[:, 4]], tbl_5[ids[:, 5]], tbl_6[ids[:, 6]], tbl_7[ids[:, 7]], tbl_8[ids[:, 8]], tbl_9[ids[:, 9]], tbl_10[ids[:, 10]], tbl_11[ids[:, 11]], tbl_12[ids[:, 12]], tbl_13[ids[:, 13]], tbl_14[ids[:, 14]], tbl_15[ids[:, 15]], tbl_16[ids[:, 16]], tbl_17[ids[:, 17]], tbl_18[ids[:, 18]], tbl_19[ids[:, 19]], tbl_20[ids[:, 20]], tbl_21[ids[:, 21]], tbl_22[ids[:, 22]], tbl_23[ids[:, 23]], tbl_24[ids[:, 24]], tbl_25[ids[:, 25]]], axis=1)
    z = _L0_rec_ref(r_dense, e)
    z = z.reshape(z.shape[0], -1)
    h = jnp.concatenate([z, r_dense], axis=1)
    h = jnp.maximum(h @ W_top1 + b_top1, 0.0)
    h = jnp.maximum(h @ W_top2 + b_top2, 0.0)
    y = h @ W_top3
    return y

_drawn_inputs = setup_inputs


def setup_inputs(seed=0):
    import zlib

    import numpy as np

    out = dict(_drawn_inputs(seed))
    spreads = {'b_top1': (0.0, 0.1), 'b_top2': (0.0, 0.1)}
    factors = {}
    for name, (base, spread) in spreads.items():
        noise = np.random.default_rng([zlib.crc32(name.encode()), seed]).standard_normal(out[name].shape)
        drawn = base * np.exp(spread * noise) if base else spread * noise
        out[name] = jnp.asarray(drawn.astype(out[name].dtype))
    for name, factor in factors.items():
        out[name] = (out[name] * factor).astype(out[name].dtype)
    return out
```

```python
from contextlib import ExitStack

import concourse.bass as bass
from concourse import mybir

F32 = mybir.dt.float32
I32 = mybir.dt.int32
ALU = mybir.AluOpType
ACT = mybir.ActivationFunctionType

P = 128
B = 512
D = 128
NT = B // P
NF = 26
NV = NF + 1
SLOT = 32
Q = P // SLOT
NG = P // Q
NJ = -(-NV // Q)
N1, N2 = 512, 256
C1, C2 = N1 // P, N2 // P
TC = 4
BATCH = 8
NB = NG // BATCH


def build(nc, ids, dense, tables, w1z, w1d, b1, w2, b2, w3, out):
    chunks = [list(range(f, min(f + TC, NF))) for f in range(0, NF, TC)]
    NC = len(chunks)

    with ExitStack() as ctx:
        def sb(name, shape, dt=F32):
            return ctx.enter_context(nc.sbuf_tensor(name, shape, dt))

        def ps(name, shape):
            return ctx.enter_context(nc.psum_tensor(name, shape, F32))

        def sem(name):
            return ctx.enter_context(nc.semaphore(name))

        idx = sb("idx", [P, NT, NF], I32)
        ident = sb("ident", [P, P])
        dn = sb("dn", [P, NT, D])
        rows = sb("rows", [P, NT, NF, D])
        vec = sb("vec", [P, NT, NG, Q, SLOT])
        dnT = sb("dnT", [P, B])
        zT = sb("zT", [P, NT, NJ, P])
        h1 = sb("h1", [P, C1, P])
        h2 = sb("h2", [P, C2, P])
        y = sb("y", [1, B])
        w1z_s = sb("w1z_s", [P, NJ, N1])
        w1d_s = sb("w1d_s", [P, N1])
        w2_s = sb("w2_s", [P, C1, N2])
        w3_s = sb("w3_s", [P, C2])
        b1_s = sb("b1_s", [P, C1])
        b2_s = sb("b2_s", [P, C2])

        pT = [ps(f"pT{i}", [P, TC, P]) for i in range(2)]
        pZ = [ps(f"pZ{i}", [P, BATCH, P]) for i in range(2)]
        pH = [ps(f"pH{i}", [P, 4, P]) for i in range(2)]

        ids_in = sem("ids_in")
        dense_in = sem("dense_in")
        w1_in = sem("w1_in")
        small_in = sem("small_in")
        got = [[sem(f"got{t}_{c}") for c in range(NC)] for t in range(NT)]
        id_zero = sem("id_zero")
        id_done = sem("id_done")
        padded = sem("padded")
        turned = sem("turned")
        kept = [sem("kept_dve"), sem("kept_act")]
        dnt_done = sem("dnt_done")
        dotted = sem("dotted")
        spread = [sem("spread_dve"), sem("spread_act")]
        sum1 = sem("sum1")
        act1 = [sem("act1_dve"), sem("act1_act")]
        sum2 = sem("sum2")
        act2 = [sem("act2_dve"), sem("act2_act")]
        sum3 = sem("sum3")
        y_done = sem("y_done")
        stored = sem("stored")

        def bank_of(t, c):
            return 1 + t * NC + c

        def copies_by(e, n):
            return n // 2 + 1 if e == 0 else (n + 1) // 2

        def between(t, step):
            if t + 1 == NT:
                return []
            last = NC - 1
            return {"dots": [0], "sum0": [1], "sum1": [2], "sum2": [3], "sum3": [4],
                    "end": list(range(5, last + 1))}[step]

        block = ctx.enter_context(nc.Block())

        @block.sync
        def _(sp):
            sp.dma_start(idx[:, :, :], ids).then_inc(ids_in, 16)
            sp.dma_start(w1z_s[:, :, :], w1z).then_inc(w1_in, 16)
            sp.dma_start(w1d_s[:, :], w1d).then_inc(w1_in, 16)
            sp.wait_ge(y_done, NT)
            sp.dma_start(out, y[:, :]).then_inc(stored, 16)
            sp.wait_ge(stored, 16)

        @block.gpsimd
        def _(pool):
            pool.memset(ident[:, :], 1.0).then_inc(id_zero, 1)
            pool.wait_ge(id_zero, 1)
            pool.affine_select(out=ident[:, :], in_=ident[:, :], compare_op=ALU.is_equal, fill=0.0, base=0,
                               pattern=[[-1, P]], channel_multiplier=1).then_inc(id_done, 1)
            pool.wait_ge(ids_in, 16)
            for t in range(NT):
                for c in range(NC):
                    for f in chunks[c]:
                        pool.indirect_dma_start(
                            rows[:, t, f, :], None, tables[f],
                            bass.IndirectOffsetOnAxis(ap=idx[:, t, f:f + 1], axis=0)).then_inc(got[t][c], 16)

        @block.tensor
        def _(pe):
            def turn(t, c):
                n = bank_of(t, c)
                pe.wait_ge(got[t][c], 16 * len(chunks[c]))
                if n >= 2:
                    pe.wait_ge(kept[n % 2], copies_by(n % 2, n - 2))
                if n == 2:
                    pe.wait_ge(dnt_done, 1)
                for k, f in enumerate(chunks[c]):
                    last = pe.transpose(pT[n % 2][:, k, :], rows[:, t, f, :], ident[:, :])
                last.then_inc(turned, 1)

            pe.wait_ge(id_done, 1)
            pe.wait_ge(dense_in, 16)
            for t in range(NT):
                last = pe.transpose(pT[0][:, t, :], dn[:, t, :], ident[:, :])
            last.then_inc(turned, 1)
            for c in range(NC):
                turn(0, c)
            pe.wait_ge(padded, 1)
            pe.wait_ge(w1_in, 32)
            for t in range(NT):
                if t:
                    pe.wait_ge(act2[0], t)
                    pe.wait_ge(y_done, t)
                for n in range(C1):
                    pe.matmul(pH[n // 2][:, n % 2, :], w1d_s[:, n * P:(n + 1) * P], dnT[:, t * P:(t + 1) * P],
                              start=(n % 2 == 0), stop=False, skip_group_check=True)
                for e in range(2):
                    pe.wait_ge(kept[e], copies_by(e, bank_of(t, NC - 1)))
                for b in range(NB):
                    m = t * NB + b
                    if m >= 2:
                        for e in range(2):
                            pe.wait_ge(spread[e], m - 1)
                    for g in range(BATCH):
                        v = vec[:, t, b * BATCH + g, :, :]
                        last = pe.matmul(pZ[m % 2][0:P - SLOT + NV, g, 0:Q * NV].rearrange("p (q s) -> p q s", q=Q),
                                         v.rearrange("p q s -> p (q s)")[:, 0:P - SLOT + NV], v[:, :, 0:NV],
                                         start=True, stop=True)
                    last.then_inc(dotted, 1)
                for c in between(t, "dots"):
                    turn(t + 1, c)
                for e in range(2):
                    pe.wait_ge(spread[e], (t + 1) * NB)
                for n in range(C1):
                    for j in range(NJ):
                        last = pe.matmul(pH[n // 2][:, n % 2, :], w1z_s[:, j, n * P:(n + 1) * P], zT[:, t, j, :],
                                         start=False, stop=(j == NJ - 1), skip_group_check=True)
                    if n % 2:
                        last.then_inc(sum1, 1)
                    for c in between(t, f"sum{n}"):
                        turn(t + 1, c)
                if t == 0:
                    pe.wait_ge(small_in, 64)
                for n in range(C2):
                    for k in range(C1):
                        if n == 0 and k % 2 == 0:
                            pe.wait_ge(act1[k // 2], t + 1)
                        last = pe.matmul(pH[n][:, 2, :], w2_s[:, k, n * P:(n + 1) * P], h1[:, k, :],
                                         start=(k == 0), stop=(k == C1 - 1), skip_group_check=True)
                    last.then_inc(sum2, 1)
                for k in reversed(range(C2)):
                    pe.wait_ge(act2[k], t + 1)
                for k in range(C2):
                    last = pe.matmul(pH[1][0:1, 3, :], w3_s[:, k:k + 1], h2[:, k, :],
                                     start=(k == 0), stop=(k == C2 - 1), skip_group_check=True)
                last.then_inc(sum3, 1)
                for c in between(t, "end"):
                    turn(t + 1, c)

        def copy_program(e, eng, copy, relu):
            def keep_dense():
                eng.wait_ge(turned, 1)
                copy(vec[:, :, :, :, 0].rearrange("p t g q -> p t q g"),
                     pT[0][:, :, :].rearrange("p t (q g) -> p t q g", q=Q)).then_inc(kept[e], 1)

            def keep(t, c):
                n = bank_of(t, c)
                if n % 2 != e:
                    return
                eng.wait_ge(turned, n + 1)
                s, w = 1 + c * TC, len(chunks[c])
                copy(vec[:, t, :, :, s:s + w].rearrange("p g q s -> p q g s"),
                     pT[n % 2][:, 0:w, :].rearrange("p s (q g) -> p q g s", q=Q)).then_inc(kept[e], 1)

            def spread_batch(t, b):
                m = t * NB + b
                eng.wait_ge(dotted, m + 1)
                if m == 0:
                    eng.wait_ge(padded, 1)
                for q in range(e, Q, 2):
                    for g in range(Q):
                        w = -(-(NV - g) // Q)
                        src = pZ[m % 2][SLOT * q:SLOT * q + NV, :, q * NV + g:q * NV + g + Q * (w - 1) + 1:Q]
                        s0 = q * NG + b * BATCH
                        last = copy(zT[SLOT * g:SLOT * g + NV, t, 0:w, s0:s0 + BATCH],
                                    src.rearrange("p b j -> p j b"))
                last.then_inc(spread[e], 1)

            if e == 0:
                keep_dense()
            else:
                eng.wait_ge(kept[0], 1)
                copy(dnT[:, :], pT[0][:, :, :].rearrange("p t b -> p (t b)")).then_inc(dnt_done, 1)
            for c in range(NC):
                keep(0, c)
            for t in range(NT):
                for b in range(NB):
                    spread_batch(t, b)
                for c in between(t, "dots"):
                    keep(t + 1, c)
                for n in range(C1):
                    if n == 2 * e + 1:
                        if t == 0:
                            eng.wait_ge(small_in, 64)
                        eng.wait_ge(sum1, t * 2 + e + 1)
                        for k in (2 * e, 2 * e + 1):
                            last = relu(h1[:, k, :], pH[e][:, k % 2, :], b1_s[:, k:k + 1])
                        last.then_inc(act1[e], 1)
                    for c in between(t, f"sum{n}"):
                        keep(t + 1, c)
                eng.wait_ge(sum2, t * C2 + e + 1)
                relu(h2[:, e, :], pH[e][:, 2, :], b2_s[:, e:e + 1]).then_inc(act2[e], 1)
                if e == 1:
                    eng.wait_ge(sum3, t + 1)
                    copy(y[:, t * P:(t + 1) * P], pH[1][0:1, 3, :]).then_inc(y_done, 1)
                for c in between(t, "end"):
                    keep(t + 1, c)

        @block.vector
        def _(dve):
            dve.memset(zT[:, :, :, :], 0.0)
            dve.memset(vec[:, :, :, :, NV:SLOT], 0.0).then_inc(padded, 1)
            copy_program(0, dve, dve.tensor_copy,
                         lambda o, i, bias: dve.tensor_scalar(o, i, bias, 0.0, ALU.add, ALU.max))

        @block.scalar
        def _(act):
            act.dma_start(dn[:, :, :], dense.rearrange("(t p) d -> p t d", p=P)).then_inc(dense_in, 16)
            act.dma_start(w2_s[:, :, :], w2.rearrange("(k p) n -> p k n", p=P)).then_inc(small_in, 16)
            act.dma_start(w3_s[:, :], w3).then_inc(small_in, 16)
            act.dma_start(b1_s[:, :], b1).then_inc(small_in, 16)
            act.dma_start(b2_s[:, :], b2).then_inc(small_in, 16)
            copy_program(1, act, lambda o, i: act.activation(o, i, ACT.Copy),
                         lambda o, i, bias: act.activation(o, i, ACT.Relu, bias=bias))


def kernel(**inputs):
    import numpy as np
    import concourse.bacc as bacc
    from concourse.bass_utils import run_bass_kernel_spmd as run

    x = {k: np.ascontiguousarray(v) for k, v in inputs.items()}
    w = x["W_top1"]
    npair = NV * (NV - 1) // 2
    pair = {}
    for i in range(NV):
        for j in range(i + 1, NV):
            pair[i, j] = len(pair)
    w1z = np.zeros((P, NJ, N1), w.dtype)
    for (i, j), r in pair.items():
        w1z[SLOT * (j % Q) + i, j // Q] = w[r]
    arrays = {
        "ids": np.ascontiguousarray(x["ids"].reshape(NT, P, NF).transpose(1, 0, 2)),
        "dense": x["r_dense"],
        "w1z": w1z,
        "w1d": np.ascontiguousarray(w[npair:]),
        "b1": np.ascontiguousarray(x["b_top1"].reshape(C1, P).T),
        "w2": x["W_top2"],
        "b2": np.ascontiguousarray(x["b_top2"].reshape(C2, P).T),
        "w3": np.ascontiguousarray(x["W_top3"].reshape(C2, P).T),
    }
    for f in range(NF):
        arrays[f"tbl_{f}"] = x[f"tbl_{f}"]
    nc = bacc.Bacc("TRN2", target_bir_lowering=False, num_devices=1)
    ap = {k: nc.dram_tensor(k, a.shape, mybir.dt.from_np(a.dtype), kind="ExternalInput").ap()
          for k, a in arrays.items()}
    out = nc.dram_tensor("out", (B, 1), F32, kind="ExternalOutput").ap()
    build(nc, ap["ids"], ap["dense"], [ap[f"tbl_{f}"] for f in range(NF)], ap["w1z"], ap["w1d"], ap["b1"],
          ap["w2"], ap["b2"], ap["w3"], out.rearrange("b o -> o b"))
    return run(nc, [arrays], core_ids=[0]).results[0]["out"]
```

```python
from contextlib import ExitStack

import concourse.bass as bass
from concourse import mybir

F32 = mybir.dt.float32
F32R = mybir.dt.float32r
I32 = mybir.dt.int32
ALU = mybir.AluOpType
ACT = mybir.ActivationFunctionType

P = 128
B = 512
D = 128
NT = B // P
NF = 26
NH = 7
NL = NF - NH
HR = 8
NV = NF + 1
SLOT = 32
Q = P // SLOT
NG = P // Q
NJ = -(-NV // Q)
N1, N2 = 512, 256
C1, C2 = N1 // P, N2 // P
TC = 4
HA = 1
HD = HR - HA
RING = 6
RAW = 4
BATCH = 8
NB = NG // BATCH


def build(nc, ids, ids_small, row_of, dense, small, tables, w1z, w1d, b1, w2, b2, w3, out):
    chunks = [list(range(f, min(f + TC, NL))) for f in range(0, NL, TC)]
    NC = len(chunks)
    PS = small[0].shape[0] // HR

    with ExitStack() as ctx:
        def sb(name, shape, dt=F32):
            return ctx.enter_context(nc.sbuf_tensor(name, shape, dt))

        def ps(name, shape):
            return ctx.enter_context(nc.psum_tensor(name, shape, F32))

        def sem(name):
            return ctx.enter_context(nc.semaphore(name))

        idx = sb("idx", [P, NT, NL], I32)
        ids_all = sb("ids_all", [PS, NH, B], I32)
        row_s = sb("row_s", [PS, 2, HR])
        ident = sb("ident", [P, P])
        dn = sb("dn", [P, NT, D])
        rows = sb("rows", [P, NT, NL, D])
        high = sb("high", [PS, 2, HR, D], F32R)
        low = sb("low", [PS, 2, HR, D], F32R)
        hot = sb("hot", [PS, RING, B], F32R)
        hot_a = sb("hot_a", [PS, 2, B], F32R)
        away = sb("away", [PS, 2, B])
        vec = sb("vec", [P, NT, NG, Q, SLOT])
        dnT = sb("dnT", [P, B])
        zT = sb("zT", [P, NT, NJ, P])
        h1 = sb("h1", [P, C1, P])
        h2 = sb("h2", [P, C2, P])
        y = sb("y", [1, B])
        w1z_s = sb("w1z_s", [P, NJ, N1])
        w1d_s = sb("w1d_s", [P, N1])
        w2_s = sb("w2_s", [P, C1, N2])
        w3_s = sb("w3_s", [P, C2])
        b1_s = sb("b1_s", [P, C1])
        b2_s = sb("b2_s", [P, C2])

        pT = [ps(f"pT{i}", [P, TC, P]) for i in range(2)]
        pZ = [ps(f"pZ{i}", [P, BATCH, P]) for i in range(2)]
        pH = [ps(f"pH{i}", [P, 4, P]) for i in range(2)]

        def raw(o):
            return rows[0:PS, NT - 2 + o // 2 % 2, HR * (o % 2):HR * (o % 2 + 1), :]

        def pick(o):
            return pZ[o // 2 % 2][:, 4 * (o % 2):4 * (o % 2) + 4, :].rearrange("p a b -> p (a b)")

        ids_in = sem("ids_in")
        ids_0_in = sem("ids_0_in")
        ids_all_in = sem("ids_all_in")
        row_in = sem("row_in")
        raw_in = [sem(f"raw_in{i}") for i in range(RAW)]
        high_done = sem("high_done")
        low_done = sem("low_done")
        hot_done = sem("hot_done")
        away_done = sem("away_done")
        hot_a_done = sem("hot_a_done")
        picked = sem("picked")
        pick_kept = sem("pick_kept")
        dense_in = sem("dense_in")
        w1_in = sem("w1_in")
        small_in = sem("small_in")
        got = [[sem(f"got{t}_{c}") for c in range(NC)] for t in range(NT)]
        id_zero = sem("id_zero")
        id_done = sem("id_done")
        padded = sem("padded")
        cleared = sem("cleared")
        turned = sem("turned")
        kept = [sem("kept_dve"), sem("kept_act")]
        dotted = sem("dotted")
        spread = [sem("spread_dve"), sem("spread_act")]
        sum1 = sem("sum1")
        act1 = [sem("act1_dve"), sem("act1_act")]
        sum2 = sem("sum2")
        act2 = [sem("act2_dve"), sem("act2_act")]
        sum3 = sem("sum3")
        y_done = sem("y_done")
        stored = sem("stored")

        def bank_of(t, c):
            return 1 + t * NC + c

        def copier(n):
            return 1 if n <= NC else n % 2

        def copies_by(e, n):
            return sum(copier(m) == e for m in range(n + 1))

        def between(t, n):
            return [c for c in range(NC) if min(c, C1 - 1) == n] if t + 1 < NT else []

        def early(o):
            return [c for c in range(NC) if min(c + 1, NH - 1) == o]

        block = ctx.enter_context(nc.Block())

        @block.sync
        def _(sp):
            sp.dma_start(idx[:, :, :], ids).then_inc(ids_in, 16)
            sp.dma_start(ids_all[:, 0:1, :], ids_small[:, 0:1, :].broadcast_to([PS, 1, B])).then_inc(ids_0_in, 16)
            sp.dma_start(dn[:, :, :], dense.rearrange("(t p) d -> p t d", p=P)).then_inc(dense_in, 16)
            for o in range(1, NH):
                if o >= RAW:
                    sp.wait_ge(low_done, o - RAW + 1)
                sp.dma_start(raw(o), small[o].rearrange("(p r) d -> p r d", r=HR)).then_inc(raw_in[o % RAW], 16)
                if o == 1:
                    sp.dma_start(ids_all[:, 1:NH, :],
                                 ids_small[:, 1:NH, :].broadcast_to([PS, NH - 1, B])).then_inc(ids_all_in, 16)
            sp.dma_start(w1z_s[:, :, :], w1z).then_inc(w1_in, 16)
            sp.dma_start(w1d_s[:, :], w1d).then_inc(w1_in, 16)
            sp.dma_start(w2_s[:, :, :], w2.rearrange("(k p) n -> p k n", p=P)).then_inc(small_in, 16)
            sp.dma_start(w3_s[:, :], w3).then_inc(small_in, 16)
            sp.dma_start(b1_s[:, :], b1).then_inc(small_in, 16)
            sp.dma_start(b2_s[:, :], b2).then_inc(small_in, 16)
            sp.wait_ge(y_done, NT)
            sp.dma_start(out, y[:, :]).then_inc(stored, 16)
            sp.wait_ge(stored, 16)

        @block.gpsimd
        def _(pool):
            pool.memset(ident[:, :], 1.0).then_inc(id_zero, 1)
            pool.wait_ge(id_zero, 1)
            pool.affine_select(out=ident[:, :], in_=ident[:, :], compare_op=ALU.is_equal, fill=0.0, base=0,
                               pattern=[[-1, P]], channel_multiplier=1).then_inc(id_done, 1)
            pool.wait_ge(ids_in, 16)
            for t in range(NT):
                if t == NT - 2:
                    pool.wait_ge(low_done, NH)
                for c in range(NC):
                    for f in chunks[c]:
                        pool.indirect_dma_start(
                            rows[:, t, f, :], None, tables[f],
                            bass.IndirectOffsetOnAxis(ap=idx[:, t, f:f + 1], axis=0)).then_inc(got[t][c], 16)

        @block.tensor
        def _(pe):
            def turn(t, c):
                n = bank_of(t, c)
                pe.wait_ge(got[t][c], 16 * len(chunks[c]))
                if n >= 2:
                    e = copier(n - 2)
                    pe.wait_ge(kept[e], copies_by(e, n - 2))
                for k, f in enumerate(chunks[c]):
                    last = pe.transpose(pT[n % 2][:, k, :], rows[:, t, f, :], ident[:, :])
                last.then_inc(turned, 1)

            def pick_rows(o):
                if o >= 4:
                    pe.wait_ge(pick_kept, o - 3)
                pe.wait_ge(low_done, o + 1)
                for k in range(HR):
                    if k < HD:
                        pe.wait_ge(hot_done, o * HD + k + 1)
                        block = hot[:, (o * HD + k) % RING, :]
                    else:
                        pe.wait_ge(hot_a_done, o * HA + k - HD + 1)
                        block = hot_a[:, (o * HA + k - HD) % 2, :]
                    for part in (high, low):
                        last = pe.matmul(pick(o), part[:, o % 2, k, :], block,
                                         start=(k == 0 and part is high), stop=(k == HR - 1 and part is low))
                    last.then_inc(picked, 1)

            def dots(t, b):
                m = t * NB + b
                if b == 0:
                    for e in range(2):
                        pe.wait_ge(kept[e], copies_by(e, bank_of(t, NC - 1)))
                if m == 0:
                    pe.wait_ge(pick_kept, NH)
                    pe.wait_ge(padded, 1)
                if m >= 2:
                    for e in range(2):
                        pe.wait_ge(spread[e], m - 1)
                for g in range(BATCH):
                    v = vec[:, t, b * BATCH + g, :, :]
                    last = pe.matmul(pZ[m % 2][0:P - SLOT + NV, g, 0:Q * NV].rearrange("p (q s) -> p q s", q=Q),
                                     v.rearrange("p q s -> p (q s)")[:, 0:P - SLOT + NV], v[:, :, 0:NV],
                                     start=True, stop=True)
                last.then_inc(dotted, 1)

            def layer1_dense(t):
                if t == 0:
                    pe.wait_ge(w1_in, 32)
                else:
                    pe.wait_ge(act2[0], t)
                    pe.wait_ge(y_done, t)
                for n in range(C1):
                    pe.matmul(pH[n // 2][:, n % 2, :], w1d_s[:, n * P:(n + 1) * P], dnT[:, t * P:(t + 1) * P],
                              start=(n % 2 == 0), stop=False, skip_group_check=True)

            def layer1(t, n):
                if n == 0:
                    for e in range(2):
                        pe.wait_ge(spread[e], (t + 1) * NB)
                for j in range(NJ):
                    last = pe.matmul(pH[n // 2][:, n % 2, :], w1z_s[:, j, n * P:(n + 1) * P], zT[:, t, j, :],
                                     start=False, stop=(j == NJ - 1), skip_group_check=True)
                if n % 2:
                    last.then_inc(sum1, 1)

            def layer2(t, n):
                if n == 0 and t == 0:
                    pe.wait_ge(small_in, 64)
                for k in range(C1):
                    if n == 0 and k % 2 == 0:
                        pe.wait_ge(act1[k // 2], t + 1)
                    last = pe.matmul(pH[n][:, 2, :], w2_s[:, k, n * P:(n + 1) * P], h1[:, k, :],
                                     start=(k == 0), stop=(k == C1 - 1), skip_group_check=True)
                last.then_inc(sum2, 1)

            def layer3(t):
                for k in reversed(range(C2)):
                    pe.wait_ge(act2[k], t + 1)
                for k in range(C2):
                    last = pe.matmul(pH[1][0:1, 3, :], w3_s[:, k:k + 1], h2[:, k, :],
                                     start=(k == 0), stop=(k == C2 - 1), skip_group_check=True)
                last.then_inc(sum3, 1)

            pe.wait_ge(id_done, 1)
            pe.wait_ge(dense_in, 16)
            for t in range(NT):
                last = pe.transpose(pT[0][:, t, :], dn[:, t, :], ident[:, :])
            last.then_inc(turned, 1)
            for o in range(NH):
                pick_rows(o)
                for c in early(o):
                    turn(0, c)
            for t in range(NT):
                dots(t, 0)
                if t:
                    layer2(t - 1, 0)
                dots(t, 1)
                if t:
                    layer2(t - 1, 1)
                dots(t, 2)
                if t:
                    layer3(t - 1)
                dots(t, 3)
                layer1_dense(t)
                for n in range(C1):
                    for c in between(t, n):
                        turn(t + 1, c)
                    layer1(t, n)
                for c in between(t, C1):
                    turn(t + 1, c)
            for n in range(C2):
                layer2(NT - 1, n)
            layer3(NT - 1)

        def spread_parts(m, t, b, quadrants):
            for q in quadrants:
                for g in range(Q):
                    w = -(-(NV - g) // Q)
                    at = q * NG + b * BATCH
                    yield (zT[SLOT * g:SLOT * g + NV, t, 0:w, at:at + BATCH],
                           pZ[m % 2][SLOT * q:SLOT * q + NV, :, q * NV + g:q * NV + g + Q * (w - 1) + 1:Q]
                           .rearrange("p b j -> p j b"))

        def places(t, c):
            s, w = 1 + NH + c * TC, len(chunks[c])
            return (vec[:, t, :, :, s:s + w].rearrange("p g q s -> p q g s"),
                    pT[bank_of(t, c) % 2][:, 0:w, :].rearrange("p s (q g) -> p q g s", q=Q))

        @block.vector
        def _(dve):
            def keep(t, c):
                n = bank_of(t, c)
                if copier(n) == 0:
                    dve.wait_ge(turned, n + 1)
                    to, of = places(t, c)
                    dve.tensor_copy(to, of).then_inc(kept[0], 1)

            def split_low(o):
                dve.wait_ge(high_done, o + 1)
                if o >= 2:
                    dve.wait_ge(picked, (o - 1) * HR)
                dve.tensor_tensor(low[:, o % 2, :, :], raw(o), high[:, o % 2, :, :].bitcast(F32),
                                  ALU.subtract).then_inc(low_done, 1)

            def spread_batch(t, b):
                m = t * NB + b
                dve.wait_ge(dotted, m + 1)
                if m == 0:
                    dve.wait_ge(cleared, NT)
                for to, of in spread_parts(m, t, b, (0, 2)):
                    last = dve.tensor_copy(to, of)
                last.then_inc(spread[0], 1)

            def relu1(t):
                if t == 0:
                    dve.wait_ge(small_in, 64)
                dve.wait_ge(sum1, 2 * t + 1)
                for k in range(2):
                    last = dve.tensor_scalar(h1[:, k, :], pH[0][:, k, :], b1_s[:, k:k + 1], 0.0, ALU.add, ALU.max)
                last.then_inc(act1[0], 1)

            def relu2(t):
                dve.wait_ge(sum2, 2 * t + 1)
                dve.tensor_scalar(h2[:, 0, :], pH[0][:, 2, :], b2_s[:, 0:1], 0.0, ALU.add,
                                  ALU.max).then_inc(act2[0], 1)

            dve.memset(vec[:, :, :, :, NV:SLOT], 0.0).then_inc(padded, 1)
            dve.wait_ge(row_in, 16)
            dve.wait_ge(ids_0_in, 16)
            for o in range(NH):
                if o == 1:
                    dve.wait_ge(ids_all_in, 16)
                for k in range(HD):
                    if k == HD // 2:
                        split_low(o)
                    n = o * HD + k
                    if n >= RING:
                        before = n - RING
                        dve.wait_ge(picked, before // HD * HR + before % HD + 1)
                    dve.tensor_scalar(hot[:, n % RING, :], ids_all[:, o, :], row_s[:, 0, k:k + 1], None,
                                      ALU.is_equal).then_inc(hot_done, 1)
            for t in range(NT):
                spread_batch(t, 0)
                if t:
                    relu2(t - 1)
                spread_batch(t, 1)
                spread_batch(t, 2)
                spread_batch(t, 3)
                for n in range(C1):
                    for c in between(t, n):
                        keep(t + 1, c)
                    if n == 1:
                        relu1(t)
                for c in between(t, C1):
                    keep(t + 1, c)
            relu2(NT - 1)

        @block.scalar
        def _(act):
            def copy(to, of):
                return act.activation(to, of, ACT.Copy)

            def keep(t, c):
                n = bank_of(t, c)
                if copier(n) == 1:
                    act.wait_ge(turned, n + 1)
                    copy(*places(t, c)).then_inc(kept[1], 1)

            def split_high(o):
                act.wait_ge(raw_in[o % RAW], 16 * (o // RAW + 1))
                if o >= 2:
                    act.wait_ge(picked, (o - 1) * HR)
                copy(high[:, o % 2, :, :], raw(o)).then_inc(high_done, 1)

            def one_hot(o):
                for k in range(HA):
                    n = o * HA + k
                    if n >= 2:
                        act.wait_ge(picked, (n - 2) // HA * HR + HD + (n - 2) % HA + 1)
                    act.activation(away[:, n % 2, :], ids_all[:, o, :], ACT.Abs,
                                   bias=row_s[:, 1, HD + k:HD + k + 1]).then_inc(away_done, 1)
                    act.wait_ge(away_done, n + 1)
                    act.activation(hot_a[:, n % 2, :], away[:, n % 2, :], ACT.Relu, bias=1.0,
                                   scale=-1.0).then_inc(hot_a_done, 1)

            def spread_batch(t, b):
                m = t * NB + b
                act.wait_ge(dotted, m + 1)
                for to, of in spread_parts(m, t, b, (1, 3)):
                    last = copy(to, of)
                last.then_inc(spread[1], 1)

            def relu1(t):
                act.wait_ge(sum1, 2 * t + 2)
                for k in range(2):
                    last = act.activation(h1[:, 2 + k, :], pH[1][:, k, :], ACT.Relu, bias=b1_s[:, 2 + k:3 + k])
                last.then_inc(act1[1], 1)

            def relu2(t):
                act.wait_ge(sum2, 2 * t + 2)
                act.activation(h2[:, 1, :], pH[1][:, 2, :], ACT.Relu, bias=b2_s[:, 1:2]).then_inc(act2[1], 1)

            def keep_y(t):
                act.wait_ge(sum3, t + 1)
                copy(y[:, t * P:(t + 1) * P], pH[1][0:1, 3, :]).then_inc(y_done, 1)

            def clear(t):
                act.activation(zT[:, t, :, :], ident[:, :].unsqueeze(1).broadcast_to([P, NJ, P]), ACT.Copy,
                               scale=0.0).then_inc(cleared, 1)

            act.dma_start(raw(0), small[0].rearrange("(p r) d -> p r d", r=HR)).then_inc(raw_in[0], 16)
            act.dma_start(row_s[:, :, :], row_of).then_inc(row_in, 16)
            act.wait_ge(id_done, 1)
            clear(0)
            split_high(0)
            act.wait_ge(row_in, 16)
            act.wait_ge(ids_0_in, 16)
            one_hot(0)
            act.wait_ge(turned, 1)
            copy(dnT[:, :], pT[0][:, :, :].rearrange("p t b -> p (t b)"))
            copy(vec[:, :, :, :, 0].rearrange("p t g q -> p t q g"),
                 pT[0][:, :, :].rearrange("p t (q g) -> p t q g", q=Q)).then_inc(kept[1], 1)
            split_high(1)
            act.wait_ge(ids_all_in, 16)
            for o in range(NH):
                if o + 1 < NH:
                    one_hot(o + 1)
                act.wait_ge(picked, (o + 1) * HR)
                copy(vec[:, :, :, :, 1 + o].rearrange("p t g q -> p t q g"),
                     pick(o).rearrange("p (t q g) -> p t q g", t=NT, q=Q)).then_inc(pick_kept, 1)
                if o + 2 < NH:
                    split_high(o + 2)
                for c in early(o):
                    keep(0, c)
                if 1 <= o < NT:
                    clear(o)
            act.wait_ge(cleared, NT)
            for t in range(NT):
                spread_batch(t, 0)
                spread_batch(t, 1)
                if t:
                    relu2(t - 1)
                spread_batch(t, 2)
                if t:
                    keep_y(t - 1)
                spread_batch(t, 3)
                for n in range(C1):
                    for c in between(t, n):
                        keep(t + 1, c)
                    if n == 3:
                        if t == 0:
                            act.wait_ge(small_in, 64)
                        relu1(t)
                for c in between(t, C1):
                    keep(t + 1, c)
            relu2(NT - 1)
            keep_y(NT - 1)


def kernel(**inputs):
    import numpy as np
    import concourse.bacc as bacc
    from concourse.bass_utils import run_bass_kernel_spmd as run

    order = sorted(range(NF), key=lambda f: inputs[f"tbl_{f}"].shape[0])
    small, large = sorted(order[:NH]), sorted(order[NH:])
    assert len({inputs[f"tbl_{f}"].shape[0] for f in small}) == 1
    ps = inputs[f"tbl_{small[0]}"].shape[0] // HR

    x = {k: np.ascontiguousarray(v) for k, v in inputs.items()}
    w = x["W_top1"]
    npair = NV * (NV - 1) // 2
    pair = {}
    slot = [0] + [1 + (small + large).index(f) for f in range(NF)]
    for i in range(NV):
        for j in range(i + 1, NV):
            pair[min(slot[i], slot[j]), max(slot[i], slot[j])] = len(pair)
    w1z = np.zeros((P, NJ, N1), w.dtype)
    for (i, j), r in pair.items():
        w1z[SLOT * (j % Q) + i, j // Q] = w[r]
    row_of = np.arange(ps * HR, dtype=np.float32).reshape(ps, HR)
    arrays = {
        "ids": np.ascontiguousarray(x["ids"][:, large].reshape(NT, P, NL).transpose(1, 0, 2)),
        "ids_small": np.ascontiguousarray(x["ids"][:, small].T)[None],
        "row_of": np.stack([row_of, -row_of], axis=1),
        "dense": x["r_dense"],
        "w1z": w1z,
        "w1d": np.ascontiguousarray(w[npair:]),
        "b1": np.ascontiguousarray(x["b_top1"].reshape(C1, P).T),
        "w2": x["W_top2"],
        "b2": np.ascontiguousarray(x["b_top2"].reshape(C2, P).T),
        "w3": np.ascontiguousarray(x["W_top3"].reshape(C2, P).T),
    }
    for f in range(NF):
        arrays[f"tbl_{f}"] = x[f"tbl_{f}"]
    nc = bacc.Bacc("TRN2", target_bir_lowering=False, num_devices=1)
    ap = {k: nc.dram_tensor(k, a.shape, mybir.dt.from_np(a.dtype), kind="ExternalInput").ap()
          for k, a in arrays.items()}
    out = nc.dram_tensor("out", (B, 1), F32, kind="ExternalOutput").ap()
    build(nc, ap["ids"], ap["ids_small"], ap["row_of"], ap["dense"], [ap[f"tbl_{f}"] for f in small],
          [ap[f"tbl_{f}"] for f in large], ap["w1z"], ap["w1d"], ap["b1"],
          ap["w2"], ap["b2"], ap["w3"], out.rearrange("b o -> o b"))
    return run(nc, [arrays], core_ids=[0]).results[0]["out"]
```

```python
from contextlib import ExitStack

import concourse.bass as bass
from concourse import mybir

F32 = mybir.dt.float32
F32R = mybir.dt.float32r
I32 = mybir.dt.int32
ALU = mybir.AluOpType
ACT = mybir.ActivationFunctionType

P = 128
B = 512
D = 128
NT = B // P
NF = 26
NH = 9
NL = NF - NH
HR = 8
NV = NF + 1
QP = 32
Q = P // QP
NG = P // Q
NR = NV - 3
VECTOR = [r if r < NR else NR + (r - NR) % 3 for r in range(QP)]
NPLACE = NR // 2
NJ = NPLACE // Q
NX = 2
N1, N2 = 512, 256
C1, C2 = N1 // P, N2 // P
TC = 4
ACT_TWICE = (5, 7)
BLOCKS = [(o, k) for o in range(NH) for k in range(HR)]
ACT_BLOCKS = [(o, k) for o, k in BLOCKS if k >= HR - (2 if o in ACT_TWICE else 1)]
DVE_BLOCKS = [x for x in BLOCKS if x not in ACT_BLOCKS]
RING = 6
RING_A = 4
RAW = 4
WARM = 13


def fold():
    odd, third, where = set(), set(), {}
    for k in range(NPLACE):
        for row, i in enumerate(VECTOR):
            if row >= NR + 6:
                x = (k - Q + 1) // Q
                j = NR + 1 + x
                if k % Q != Q - 1 or x >= NX or i == j:
                    continue
                third.add((k, row))
            elif row >= NR:
                j = 2 * k + (row - NR) // 3
            elif i // 2 != k:
                j = 2 * k + (i % 2 if i // 2 > k else 1 - i % 2)
            elif i % 2:
                j = 2 * k
            else:
                continue
            if j < NR and j % 2:
                odd.add((k, row))
            assert (min(i, j), max(i, j)) not in where
            where[min(i, j), max(i, j)] = (k, row)
    assert len(where) == NV * (NV - 1) // 2
    return odd, third, where


def build(nc, ids, ids_small, row_of, take, dense, small, tables, w1z, w1d, b1, w2, b2, w3, out):
    chunks = [list(range(f, min(f + TC, NL))) for f in range(0, NL, TC)]
    NC = len(chunks)
    PS = small[0].shape[0] // HR

    with ExitStack() as ctx:
        def sb(name, shape, dt=F32):
            return ctx.enter_context(nc.sbuf_tensor(name, shape, dt))

        def ps(name, shape):
            return ctx.enter_context(nc.psum_tensor(name, shape, F32))

        def sem(name):
            return ctx.enter_context(nc.semaphore(name))

        idx = sb("idx", [P, NT, NL], I32)
        ids_all = sb("ids_all", [PS, NH, B], I32)
        row_s = sb("row_s", [PS, 2, HR])
        ident = sb("ident", [P, P])
        dn = sb("dn", [P, NT, D])
        rows = sb("rows", [P, NT, NL, D])
        high = sb("high", [PS, 2, HR, D], F32R)
        low = sb("low", [PS, 2, HR, D], F32R)
        hot = sb("hot", [PS, RING, B], F32R)
        hot_a = sb("hot_a", [PS, RING_A, B], F32R)
        away = sb("away", [PS, RING_A, B])
        vec = sb("vec", [P, NT, P, QP])
        dnT = sb("dnT", [P, B])
        zT = sb("zT", [P, NT, NJ, P])
        take_s = sb("take_s", [P, NJ + NX], I32)
        h1 = sb("h1", [P, C1, P])
        h2 = sb("h2", [P, C2, P])
        y = sb("y", [1, B])
        w1z_s = sb("w1z_s", [P, NJ, N1])
        w1d_s = sb("w1d_s", [P, N1])
        w2_s = sb("w2_s", [P, C1, N2])
        w3_s = sb("w3_s", [P, C2])
        b1_s = sb("b1_s", [P, C1])
        b2_s = sb("b2_s", [P, C2])

        pT = [ps(f"pT{i}", [P, TC, P]) for i in range(2)]
        pZ = ps("pZ", [P, NG, QP])
        pH = [ps(f"pH{i}", [P, 4, P]) for i in range(2)]
        pG = [ps(f"pG{i}", [P, 4, P]) for i in range(2)]

        def raw(o):
            return rows[0:PS, NT - 2 + o // 2 % 2, HR * (o % 2):HR * (o % 2 + 1), :]

        def pick(o):
            banks = [pZ[:, 0:NG // 2, :], pZ[:, NG // 2:NG, :], pG[1]]
            return banks[o % 3].rearrange("p a b -> p (a b)")

        ids_in = sem("ids_in")
        ids_all_in = [sem(f"ids_all_in{o}") for o in range(NH)]
        row_in = sem("row_in")
        raw_in = [sem(f"raw_in{i}") for i in range(RAW)]
        dense_in = sem("dense_in")
        take_in = sem("take_in")
        w1_in = sem("w1_in")
        small_in = sem("small_in")
        got = [[sem(f"got{t}_{c}") for c in range(NC)] for t in range(NT)]
        stored = sem("stored")
        id_zero = sem("id_zero")
        id_done = sem("id_done")
        high_done = sem("high_done")
        low_done = sem("low_done")
        hot_done = sem("hot_done")
        away_done = sem("away_done")
        hot_a_done = sem("hot_a_done")
        picked = sem("picked")
        pick_kept = sem("pick_kept")
        turned = sem("turned")
        kept = [sem("kept_dve"), sem("kept_act")]
        dotted = sem("dotted")
        even_done = sem("even_done")
        odd_done = sem("odd_done")
        spread = sem("spread")
        sum1 = sem("sum1")
        act1 = [sem("act1_dve"), sem("act1_act")]
        sum2 = sem("sum2")
        act2 = [sem("act2_dve"), sem("act2_act")]
        sum3 = sem("sum3")
        y_done = sem("y_done")

        def bank_of(t, c):
            return 1 + t * NC + c

        def copier(n):
            return 1 if n <= NC else n % 2

        def copies_by(e, n):
            return sum(copier(m) == e for m in range(n + 1))

        def between(t, n):
            if t == NT - 1:
                return []
            return [c for c in range(NC) if n == (-2 if t == c == 0 else max(c - (2 if t else 3), -1))]

        def early(o):
            return [c for c in range(NC) if min(c + 1, NH - 1) == o]

        block = ctx.enter_context(nc.Block())

        @block.sync
        def _(sp):
            sp.dma_start(idx[:, :, :], ids).then_inc(ids_in, 16)
            for o in range(NH):
                sp.dma_start(ids_all[:, o:o + 1, :],
                             ids_small[:, o:o + 1, :].broadcast_to([PS, 1, B])).then_inc(ids_all_in[o], 16)
                if o >= RAW:
                    sp.wait_ge(low_done, o - RAW + 1)
                if o:
                    sp.dma_start(raw(o), small[o].rearrange("(p r) d -> p r d", r=HR)).then_inc(raw_in[o % RAW], 16)
                if o == 1:
                    sp.dma_start(dn[:, :, :], dense.rearrange("(t p) d -> p t d", p=P)).then_inc(dense_in, 16)
            sp.dma_start(take_s[:, :], take).then_inc(take_in, 16)
            sp.dma_start(w1z_s[:, :, :], w1z).then_inc(w1_in, 16)
            sp.dma_start(w1d_s[:, :], w1d).then_inc(w1_in, 16)
            sp.dma_start(w2_s[:, :, :], w2.rearrange("(k p) n -> p k n", p=P)).then_inc(small_in, 16)
            sp.dma_start(w3_s[:, :], w3).then_inc(small_in, 16)
            sp.dma_start(b1_s[:, :], b1).then_inc(small_in, 16)
            sp.dma_start(b2_s[:, :], b2).then_inc(small_in, 16)
            sp.wait_ge(y_done, NT)
            sp.dma_start(out, y[:, :]).then_inc(stored, 16)
            sp.wait_ge(stored, 16)

        @block.gpsimd
        def _(pool):
            pool.memset(ident[:, :], 1.0).then_inc(id_zero, 1)
            pool.wait_ge(id_zero, 1)
            pool.affine_select(out=ident[:, :], in_=ident[:, :], compare_op=ALU.is_equal, fill=0.0, base=0,
                               pattern=[[-1, P]], channel_multiplier=1).then_inc(id_done, 1)
            pool.wait_ge(ids_in, 16)
            for t in range(NT):
                if t == NT - 2:
                    pool.wait_ge(low_done, NH)
                for c in range(NC):
                    for f in chunks[c]:
                        pool.indirect_dma_start(
                            rows[:, t, f, :], None, tables[f],
                            bass.IndirectOffsetOnAxis(ap=idx[:, t, f:f + 1], axis=0)).then_inc(got[t][c], 16)

        @block.tensor
        def _(pe):
            def turn(t, c):
                n = bank_of(t, c)
                pe.wait_ge(got[t][c], 16 * len(chunks[c]))
                if n >= 2:
                    e = copier(n - 2)
                    pe.wait_ge(kept[e], copies_by(e, n - 2))
                for k, f in enumerate(chunks[c]):
                    last = pe.transpose(pT[n % 2][:, k, :], rows[:, t, f, :], ident[:, :])
                last.then_inc(turned, 1)

            def pick_rows(o):
                if o >= 3:
                    pe.wait_ge(pick_kept, o - 2)
                pe.wait_ge(low_done, o + 1)
                for k in range(HR):
                    if (o, k) in DVE_BLOCKS:
                        n = DVE_BLOCKS.index((o, k))
                        pe.wait_ge(hot_done, n + 1)
                        block = hot[:, n % RING, :]
                    else:
                        n = ACT_BLOCKS.index((o, k))
                        pe.wait_ge(hot_a_done, n + 1)
                        block = hot_a[:, n % RING_A, :]
                    for part in (high, low):
                        last = pe.matmul(pick(o), part[:, o % 2, k, :], block,
                                         start=(k == 0 and part is high), stop=(k == HR - 1 and part is low))
                    last.then_inc(picked, 1)

            def dots(t, q):
                if q == 0:
                    for e in range(2):
                        pe.wait_ge(kept[e], copies_by(e, bank_of(t, NC - 1)))
                    if t == 0:
                        pe.wait_ge(pick_kept, NH)
                if t:
                    pe.wait_ge(spread, (t - 1) * Q + q + 1)
                for g in range(NG):
                    v = vec[:, t, q * NG + g, :]
                    last = pe.matmul(pZ[QP * q:QP * (q + 1), g, 0:NV], v, v[:, 0:NV], start=True, stop=True)
                last.then_inc(dotted, 1)

            def layer1_dense(t):
                if t == 0:
                    pe.wait_ge(w1_in, 32)
                else:
                    for e in range(2):
                        pe.wait_ge(act1[e], 2 * t)
                for n in range(C1):
                    pe.matmul(pH[n // 2][:, n % 2, :], w1d_s[:, n * P:(n + 1) * P], dnT[:, t * P:(t + 1) * P],
                              start=(n % 2 == 0), stop=False, skip_group_check=True)

            def layer1(t, n):
                if n == 0:
                    pe.wait_ge(spread, (t + 1) * Q)
                for j in range(NJ):
                    last = pe.matmul(pH[n // 2][:, n % 2, :], w1z_s[:, j, n * P:(n + 1) * P], zT[:, t, j, :],
                                     start=False, stop=(j == NJ - 1), skip_group_check=True)
                if n % 2:
                    last.then_inc(sum1, 1)

            def layer2(t, half):
                if t and half == 0:
                    pe.wait_ge(act2[1], t)
                    pe.wait_ge(y_done, t)
                elif half == 0:
                    pe.wait_ge(small_in, 64)
                for k in range(C1 // 2 * half, C1 // 2 * (half + 1)):
                    pe.wait_ge(act1[k // 2], 2 * t + k % 2 + 1)
                    for n in range(C2):
                        last = pe.matmul(pG[n][:, 0, :], w2_s[:, k, n * P:(n + 1) * P], h1[:, k, :],
                                         start=(k == 0), stop=(k == C1 - 1))
                        if k == C1 - 1:
                            last.then_inc(sum2, 1)

            def layer3(t):
                for k in range(C2):
                    pe.wait_ge(act2[k], t + 1)
                    last = pe.matmul(pG[0][0:1, 1, :], w3_s[:, k:k + 1], h2[:, k, :],
                                     start=(k == 0), stop=(k == C2 - 1))
                last.then_inc(sum3, 1)

            pe.wait_ge(id_done, 1)
            for n in range(WARM):
                pe.matmul(pT[0][:, 0, :], ident[:, :], ident[:, :], start=True, stop=True)
            for o in range(NH):
                pick_rows(o)
                if o == 0:
                    pe.wait_ge(dense_in, 16)
                    for t in range(NT):
                        last = pe.transpose(pT[0][:, t, :], dn[:, t, :], ident[:, :])
                    last.then_inc(turned, 1)
                for c in early(o):
                    turn(0, c)
            for t in range(NT):
                for c in between(t, -2):
                    turn(t + 1, c)
                middle = 0 < t < NT - 1
                if t == NT - 1:
                    layer2(t - 1, 0)
                for q in range(Q):
                    dots(t, q)
                    if middle and q == 1:
                        layer1_dense(t)
                    if middle and q == 2:
                        layer2(t - 1, 0)
                if not middle:
                    layer1_dense(t)
                if t:
                    layer2(t - 1, 1)
                for c in between(t, -1):
                    turn(t + 1, c)
                for n in range(C1):
                    layer1(t, n)
                    if n == 0 and t:
                        layer3(t - 1)
                    for c in between(t, n):
                        turn(t + 1, c)
            for half in range(2):
                layer2(NT - 1, half)
            layer3(NT - 1)

        def product_part(t, q, g, odd):
            c = 2 * g + odd
            to = zT[QP * g:QP * (g + 1), t, :, q * NG:(q + 1) * NG]
            of = pZ[QP * q:QP * (q + 1), :, c:c + 2 * Q * (NJ - 1) + 1:2 * Q]
            mask = take_s[QP * g:QP * (g + 1), 0:NJ].unsqueeze(2).broadcast_to([QP, NJ, NG])
            return to, mask, of.rearrange("p b j -> p j b")

        def third_part(t, q):
            g = Q - 1
            to = zT[QP * g:QP * (g + 1), t, 0:NX, q * NG:(q + 1) * NG]
            of = pZ[QP * q:QP * (q + 1), :, NR + 1:NR + 1 + NX]
            mask = take_s[QP * g:QP * (g + 1), NJ:NJ + NX].unsqueeze(2).broadcast_to([QP, NX, NG])
            return to, mask, of.rearrange("p b j -> p j b")

        def places(t, c):
            s, w = NH - 2 + c * TC, len(chunks[c])
            return vec[:, t, :, s:s + w], pT[bank_of(t, c) % 2][:, 0:w, :].rearrange("p s b -> p b s")

        def copies(i):
            return vec[:, :, :, NR + i:QP:3].rearrange("p t b s -> p (t b) s")

        @block.vector
        def _(dve):
            def keep(t, c):
                n = bank_of(t, c)
                if copier(n) == 0:
                    dve.wait_ge(turned, n + 1)
                    to, of = places(t, c)
                    dve.tensor_copy(to, of).then_inc(kept[0], 1)

            def split_low(o):
                dve.wait_ge(high_done, o + 1)
                if o >= 2:
                    dve.wait_ge(picked, (o - 1) * HR)
                dve.tensor_tensor(low[:, o % 2, :, :], raw(o), high[:, o % 2, :, :].bitcast(F32),
                                  ALU.subtract).then_inc(low_done, 1)

            def spread_odd(t):
                if t == 0:
                    dve.wait_ge(take_in, 16)
                for q in range(Q):
                    dve.wait_ge(even_done, t * Q + q + 1)
                    dve.copy_predicated(*product_part(t, q, Q - 1, 1)).then_inc(odd_done, 1)
                    for g in range(Q - 1):
                        dve.copy_predicated(*product_part(t, q, g, 1))
                    dve.wait_ge(odd_done, t * Q + q + 1)
                    dve.copy_predicated(*third_part(t, q)).then_inc(spread, 1)

            def relu1(t):
                if t == 0:
                    dve.wait_ge(small_in, 64)
                dve.wait_ge(sum1, 2 * t + 1)
                for k in range(2):
                    dve.tensor_scalar(h1[:, k, :], pH[0][:, k, :], b1_s[:, k:k + 1], 0.0, ALU.add,
                                      ALU.max).then_inc(act1[0], 1)

            def relu2(t):
                dve.wait_ge(sum2, 2 * t + 1)
                dve.tensor_scalar(h2[:, 0, :], pG[0][:, 0, :], b2_s[:, 0:1], 0.0, ALU.add,
                                  ALU.max).then_inc(act2[0], 1)

            def keep_y(t):
                dve.wait_ge(sum3, t + 1)
                dve.tensor_copy(y[:, t * P:(t + 1) * P], pG[0][0:1, 1, :]).then_inc(y_done, 1)

            dve.wait_ge(row_in, 16)
            for o in range(NH):
                dve.wait_ge(ids_all_in[o], 16)
                for k in (k for table, k in DVE_BLOCKS if table == o):
                    n = DVE_BLOCKS.index((o, k))
                    if k == 1:
                        split_low(o)
                    if n >= RING:
                        dve.wait_ge(picked, BLOCKS.index(DVE_BLOCKS[n - RING]) + 1)
                    dve.tensor_scalar(hot[:, n % RING, :], ids_all[:, o, :], row_s[:, 0, k:k + 1], None,
                                      ALU.is_equal).then_inc(hot_done, 1)
            for t in range(NT):
                for c in between(t, -2):
                    keep(t + 1, c)
                spread_odd(t)
                if t:
                    relu2(t - 1)
                for c in between(t, -1):
                    keep(t + 1, c)
                for n in range(C1):
                    if n == 1:
                        relu1(t)
                    for c in between(t, n):
                        keep(t + 1, c)
                    if n == 0 and t:
                        keep_y(t - 1)
            relu2(NT - 1)
            keep_y(NT - 1)

        @block.scalar
        def _(act):
            def copy(to, of):
                return act.activation(to, of, ACT.Copy)

            def keep(t, c):
                n = bank_of(t, c)
                if copier(n) == 1:
                    act.wait_ge(turned, n + 1)
                    copy(*places(t, c)).then_inc(kept[1], 1)

            def split_high(o):
                act.wait_ge(raw_in[o % RAW], 16 * (o // RAW + 1))
                if o >= 2:
                    act.wait_ge(picked, (o - 1) * HR)
                copy(high[:, o % 2, :, :], raw(o)).then_inc(high_done, 1)

            def one_hot(o):
                act.wait_ge(ids_all_in[o], 16)
                for k in (k for table, k in ACT_BLOCKS if table == o):
                    n = ACT_BLOCKS.index((o, k))
                    if n >= RING_A:
                        act.wait_ge(picked, BLOCKS.index(ACT_BLOCKS[n - RING_A]) + 1)
                    act.activation(away[:, n % RING_A, :], ids_all[:, o, :], ACT.Abs,
                                   bias=row_s[:, 1, k:k + 1]).then_inc(away_done, 1)
                    act.wait_ge(away_done, n + 1)
                    act.activation(hot_a[:, n % RING_A, :], away[:, n % RING_A, :], ACT.Relu, bias=1.0,
                                   scale=-1.0).then_inc(hot_a_done, 1)

            def spread_even(t):
                for q in range(Q):
                    act.wait_ge(dotted, t * Q + q + 1)
                    for g in range(Q):
                        to, _, of = product_part(t, q, g, 0)
                        last = copy(to, of)
                    last.then_inc(even_done, 1)

            def relu1(t):
                act.wait_ge(sum1, 2 * t + 2)
                for k in range(2):
                    act.activation(h1[:, 2 + k, :], pH[1][:, k, :], ACT.Relu,
                                   bias=b1_s[:, 2 + k:3 + k]).then_inc(act1[1], 1)

            def relu2(t):
                act.wait_ge(sum2, 2 * t + 2)
                act.activation(h2[:, 1, :], pG[1][:, 0, :], ACT.Relu, bias=b2_s[:, 1:2]).then_inc(act2[1], 1)

            act.dma_start(raw(0), small[0].rearrange("(p r) d -> p r d", r=HR)).then_inc(raw_in[0], 16)
            act.dma_start(row_s[:, :, :], row_of).then_inc(row_in, 16)
            split_high(0)
            act.wait_ge(row_in, 16)
            one_hot(0)
            split_high(1)
            for o in range(NH):
                if o + 1 < NH:
                    one_hot(o + 1)
                act.wait_ge(picked, (o + 1) * HR)
                if o + 2 < NH:
                    split_high(o + 2)
                if o < 2:
                    to = copies(o)
                    copy(to, pick(o).unsqueeze(2).broadcast_to(to.shape)).then_inc(pick_kept, 1)
                else:
                    copy(vec[:, :, :, o - 2], pick(o).rearrange("p (t b) -> p t b", t=NT)).then_inc(pick_kept, 1)
                if o == 0:
                    act.wait_ge(turned, 1)
                    copy(dnT[:, :], pT[0][:, :, :].rearrange("p t b -> p (t b)"))
                    to = copies(2)
                    of = pT[0][:, :, :].rearrange("p t b -> p (t b)")
                    copy(to, of.unsqueeze(2).broadcast_to(to.shape)).then_inc(kept[1], 1)
                for c in early(o):
                    keep(0, c)
            for t in range(NT):
                for c in between(t, -2):
                    keep(t + 1, c)
                spread_even(t)
                if t == 0:
                    act.wait_ge(small_in, 64)
                else:
                    relu2(t - 1)
                for n in range(-1, C1):
                    if n == C1 - 1:
                        relu1(t)
                    for c in between(t, n):
                        keep(t + 1, c)
            relu2(NT - 1)


def kernel(**inputs):
    import numpy as np
    import concourse.bacc as bacc
    from concourse.bass_utils import run_bass_kernel_spmd as run

    order = sorted(range(NF), key=lambda f: inputs[f"tbl_{f}"].shape[0])
    small, large = sorted(order[:NH]), sorted(order[NH:])
    assert len({inputs[f"tbl_{f}"].shape[0] for f in small}) == 1
    ps = inputs[f"tbl_{small[0]}"].shape[0] // HR

    x = {k: np.ascontiguousarray(v) for k, v in inputs.items()}
    w = x["W_top1"]
    npair = NV * (NV - 1) // 2
    tables = small[2:] + large + small[:2]
    vector = [NV - 1] + [tables.index(f) for f in range(NF)]
    odd, third, where = fold()
    w1z = np.zeros((P, NJ, N1), w.dtype)
    r = 0
    for i in range(NV):
        for j in range(i + 1, NV):
            k, row = where[min(vector[i], vector[j]), max(vector[i], vector[j])]
            w1z[QP * (k % Q) + row, k // Q] = w[r]
            r += 1
    take = np.zeros((P, NJ + NX), np.int32)
    for k, row in odd:
        take[QP * (k % Q) + row, k // Q] = 1
    for k, row in third:
        take[QP * (k % Q) + row, NJ + k // Q] = 1
    row_of = np.arange(ps * HR, dtype=np.float32).reshape(ps, HR)
    arrays = {
        "ids": np.ascontiguousarray(x["ids"][:, large].reshape(NT, P, NL).transpose(1, 0, 2)),
        "ids_small": np.ascontiguousarray(x["ids"][:, small].T)[None],
        "take": take,
        "row_of": np.stack([row_of, -row_of], axis=1),
        "dense": x["r_dense"],
        "w1z": w1z,
        "w1d": np.ascontiguousarray(w[npair:]),
        "b1": np.ascontiguousarray(x["b_top1"].reshape(C1, P).T),
        "w2": x["W_top2"],
        "b2": np.ascontiguousarray(x["b_top2"].reshape(C2, P).T),
        "w3": np.ascontiguousarray(x["W_top3"].reshape(C2, P).T),
    }
    for f in range(NF):
        arrays[f"tbl_{f}"] = x[f"tbl_{f}"]
    nc = bacc.Bacc("TRN2", target_bir_lowering=False, num_devices=1)
    ap = {k: nc.dram_tensor(k, a.shape, mybir.dt.from_np(a.dtype), kind="ExternalInput").ap()
          for k, a in arrays.items()}
    out = nc.dram_tensor("out", (B, 1), F32, kind="ExternalOutput").ap()
    build(nc, ap["ids"], ap["ids_small"], ap["row_of"], ap["take"], ap["dense"], [ap[f"tbl_{f}"] for f in small],
          [ap[f"tbl_{f}"] for f in large], ap["w1z"], ap["w1d"], ap["b1"],
          ap["w2"], ap["b2"], ap["w3"], out.rearrange("b o -> o b"))
    return run(nc, [arrays], core_ids=[0]).results[0]["out"]
```
